# Optimizing a Trainium2 kernel written in Bass

```python
import numpy as np
import jax
import jax.numpy as jnp

def _softmax(x, axis=-1):
    return jax.nn.softmax(x, axis=axis)

def _gelu(x):
    return jax.nn.gelu(x, approximate=True)

def _silu(x):
    return jax.nn.silu(x)

def _sigmoid(x):
    return jax.nn.sigmoid(x)

def _layernorm(x, axis=-1, eps=1e-05):
    m = jnp.mean(x, axis=axis, keepdims=True)
    v = jnp.var(x, axis=axis, keepdims=True)
    return (x - m) / jnp.sqrt(v + eps)

def _scatter_add(tgt, idx, src, axis=0):
    return tgt.at[idx].add(src)

def _segment_sum(src, seg, n):
    return jax.ops.segment_sum(src, seg, n)
kernel_name = 'mk_dlrm_tower_d1_rec_r8_2a03e6'

def setup_inputs(seed: int=0):
    np.random.seed(seed)
    _w = jnp.asarray

    def _rec_inputs():
        import jax
        import jax.numpy as jnp
        _tk = jax.random.key(seed)
        ids = jnp.stack([jax.random.randint(jax.random.fold_in(_tk, 200 + f), (2048,), 0, v, jnp.int32) for f, v in enumerate([1000, 1000, 125000, 1000, 12500, 1250, 1000, 12500, 1000, 1000, 1250, 1250, 1000, 1000, 1250, 1000, 1250, 1000, 1000, 1250, 1250, 12500, 1250, 1000, 12500, 1000])], axis=1)
        tbl_0 = 0.05 * jax.random.normal(jax.random.fold_in(_tk, 500 + 0), (1000, 128), jnp.float32)
        tbl_1 = 0.05 * jax.random.normal(jax.random.fold_in(_tk, 500 + 1), (1000, 128), jnp.float32)
        tbl_2 = 0.05 * jax.random.normal(jax.random.fold_in(_tk, 500 + 2), (125000, 128), jnp.float32)
        tbl_3 = 0.05 * jax.random.normal(jax.random.fold_in(_tk, 500 + 3), (1000, 128), jnp.float32)
        tbl_4 = 0.05 * jax.random.normal(jax.random.fold_in(_tk, 500 + 4), (12500, 128), jnp.float32)
        tbl_5 = 0.05 * jax.random.normal(jax.random.fold_in(_tk, 500 + 5), (1250, 128), jnp.float32)
        tbl_6 = 0.05 * jax.random.normal(jax.random.fold_in(_tk, 500 + 6), (1000, 128), jnp.float32)
        tbl_7 = 0.05 * jax.random.normal(jax.random.fold_in(_tk, 500 + 7), (12500, 128), jnp.float32)
        tbl_8 = 0.05 * jax.random.normal(jax.random.fold_in(_tk, 500 + 8), (1000, 128), jnp.float32)
        tbl_9 = 0.05 * jax.random.normal(jax.random.fold_in(_tk, 500 + 9), (1000, 128), jnp.float32)
        tbl_10 = 0.05 * jax.random.normal(jax.random.fold_in(_tk, 500 + 10), (1250, 128), jnp.float32)
        tbl_11 = 0.05 * jax.random.normal(jax.random.fold_in(_tk, 500 + 11), (1250, 128), jnp.float32)
        tbl_12 = 0.05 * jax.random.normal(jax.random.fold_in(_tk, 500 + 12), (1000, 128), jnp.float32)
        tbl_13 = 0.05 * jax.random.normal(jax.random.fold_in(_tk, 500 + 13), (1000, 128), jnp.float32)
        tbl_14 = 0.05 * jax.random.normal(jax.random.fold_in(_tk, 500 + 14), (1250, 128), jnp.float32)
        tbl_15 = 0.05 * jax.random.normal(jax.random.fold_in(_tk, 500 + 15), (1000, 128), jnp.float32)
        tbl_16 = 0.05 * jax.random.normal(jax.random.fold_in(_tk, 500 + 16), (1250, 128), jnp.float32)
        tbl_17 = 0.05 * jax.random.normal(jax.random.fold_in(_tk, 500 + 17), (1000, 128), jnp.float32)
        tbl_18 = 0.05 * jax.random.normal(jax.random.fold_in(_tk, 500 + 18), (1000, 128), jnp.float32)
        tbl_19 = 0.05 * jax.random.normal(jax.random.fold_in(_tk, 500 + 19), (1250, 128), jnp.float32)
        tbl_20 = 0.05 * jax.random.normal(jax.random.fold_in(_tk, 500 + 20), (1250, 128), jnp.float32)
        tbl_21 = 0.05 * jax.random.normal(jax.random.fold_in(_tk, 500 + 21), (12500, 128), jnp.float32)
        tbl_22 = 0.05 * jax.random.normal(jax.random.fold_in(_tk, 500 + 22), (1250, 128), jnp.float32)
        tbl_23 = 0.05 * jax.random.normal(jax.random.fold_in(_tk, 500 + 23), (1000, 128), jnp.float32)
        tbl_24 = 0.05 * jax.random.normal(jax.random.fold_in(_tk, 500 + 24), (12500, 128), jnp.float32)
        tbl_25 = 0.05 * jax.random.normal(jax.random.fold_in(_tk, 500 + 25), (1000, 128), jnp.float32)
        _rk = jax.random.fold_in(_tk, 7)
        r_dense_features = 7.22013e-05 + 1.00017 * jax.random.normal(jax.random.fold_in(_rk, 101), (2048, 128), jnp.float32)
        W_top1 = 0.0456912 * jax.random.normal(jax.random.fold_in(_tk, 801), (479, 512), jnp.float32)
        W_top2 = 0.0441942 * jax.random.normal(jax.random.fold_in(_tk, 802), (512, 256), jnp.float32)
        W_top3 = 0.0625 * jax.random.normal(jax.random.fold_in(_tk, 803), (256, 1), jnp.float32)
        b_top1 = jnp.zeros((512,), jnp.float32)
        b_top2 = jnp.zeros((256,), jnp.float32)
        return (r_dense_features, ids, tbl_0, tbl_1, tbl_2, tbl_3, tbl_4, tbl_5, tbl_6, tbl_7, tbl_8, tbl_9, tbl_10, tbl_11, tbl_12, tbl_13, tbl_14, tbl_15, tbl_16, tbl_17, tbl_18, tbl_19, tbl_20, tbl_21, tbl_22, tbl_23, tbl_24, tbl_25, W_top1, b_top1, W_top2, b_top2, W_top3)
    r_dense_features, ids, tbl_0, tbl_1, tbl_2, tbl_3, tbl_4, tbl_5, tbl_6, tbl_7, tbl_8, tbl_9, tbl_10, tbl_11, tbl_12, tbl_13, tbl_14, tbl_15, tbl_16, tbl_17, tbl_18, tbl_19, tbl_20, tbl_21, tbl_22, tbl_23, tbl_24, tbl_25, W_top1, b_top1, W_top2, b_top2, W_top3 = _rec_inputs()

    def _L0_rec_setup():
        import jax, jax.numpy as jnp
        import numpy as np
        FEATURE_NUM = 27
        key = jax.random.key(seed)
        k1, k2 = jax.random.split(key)
        B, N, D = (8192, FEATURE_NUM - 1, 128)
        dense_features = jax.random.normal(k1, (B, D), dtype=jnp.float32)
        sparse_features = jax.random.normal(k2, (B, N, D), dtype=jnp.float32)
        return {'dense_features': dense_features, 'sparse_features': sparse_features}
    _L0_rec_all = _L0_rec_setup()
    _L0_rec_in = {k: v for k, v in _L0_rec_all.items() if k in ()}
    del _L0_rec_all
    return {'r_dense_features': r_dense_features, 'ids': ids, 'tbl_0': tbl_0, 'tbl_1': tbl_1, 'tbl_2': tbl_2, 'tbl_3': tbl_3, 'tbl_4': tbl_4, 'tbl_5': tbl_5, 'tbl_6': tbl_6, 'tbl_7': tbl_7, 'tbl_8': tbl_8, 'tbl_9': tbl_9, 'tbl_10': tbl_10, 'tbl_11': tbl_11, 'tbl_12': tbl_12, 'tbl_13': tbl_13, 'tbl_14': tbl_14, 'tbl_15': tbl_15, 'tbl_16': tbl_16, 'tbl_17': tbl_17, 'tbl_18': tbl_18, 'tbl_19': tbl_19, 'tbl_20': tbl_20, 'tbl_21': tbl_21, 'tbl_22': tbl_22, 'tbl_23': tbl_23, 'tbl_24': tbl_24, 'tbl_25': tbl_25, 'W_top1': W_top1, 'b_top1': b_top1, 'W_top2': W_top2, 'b_top2': b_top2, 'W_top3': W_top3}

def reference(r_dense_features, ids, tbl_0, tbl_1, tbl_2, tbl_3, tbl_4, tbl_5, tbl_6, tbl_7, tbl_8, tbl_9, tbl_10, tbl_11, tbl_12, tbl_13, tbl_14, tbl_15, tbl_16, tbl_17, tbl_18, tbl_19, tbl_20, tbl_21, tbl_22, tbl_23, tbl_24, tbl_25, W_top1, b_top1, W_top2, b_top2, W_top3):
    import jax
    import jax.numpy as jnp

    def _L0_rec_ref(dense_features, sparse_features):
        import jax, jax.numpy as jnp
        import numpy as np
        FEATURE_NUM = 27
        combined = jnp.concatenate([dense_features[:, None, :], sparse_features], axis=1)
        interactions = jnp.einsum('bfd,bgd->bfg', combined, combined)
        iu, ju = jnp.triu_indices(FEATURE_NUM, k=1)
        return interactions[:, iu, ju]
    e = jnp.stack([tbl_0[ids[:, 0]], tbl_1[ids[:, 1]], tbl_2[ids[:, 2]], tbl_3[ids[:, 3]], tbl_4[ids[:, 4]], tbl_5[ids[:, 5]], tbl_6[ids[:, 6]], tbl_7[ids[:, 7]], tbl_8[ids[:, 8]], tbl_9[ids[:, 9]], tbl_10[ids[:, 10]], tbl_11[ids[:, 11]], tbl_12[ids[:, 12]], tbl_13[ids[:, 13]], tbl_14[ids[:, 14]], tbl_15[ids[:, 15]], tbl_16[ids[:, 16]], tbl_17[ids[:, 17]], tbl_18[ids[:, 18]], tbl_19[ids[:, 19]], tbl_20[ids[:, 20]], tbl_21[ids[:, 21]], tbl_22[ids[:, 22]], tbl_23[ids[:, 23]], tbl_24[ids[:, 24]], tbl_25[ids[:, 25]]], axis=1)
    z = _L0_rec_ref(r_dense_features, e)
    z = z.reshape(z.shape[0], -1)
    h = jnp.concatenate([z, r_dense_features], axis=1)
    h = jnp.maximum(h @ W_top1 + b_top1, 0.0)
    h = jnp.maximum(h @ W_top2 + b_top2, 0.0)
    y = h @ W_top3
    return y

_drawn_inputs = setup_inputs


def setup_inputs(seed=0):
    import zlib

    import numpy as np

    out = dict(_drawn_inputs(seed))
    spreads = {'b_top1': (0.0, 0.1), 'b_top2': (0.0, 0.1)}
    factors = {}
    for name, (base, spread) in spreads.items():
        noise = np.random.default_rng([zlib.crc32(name.encode()), seed]).standard_normal(out[name].shape)
        drawn = base * np.exp(spread * noise) if base else spread * noise
        out[name] = jnp.asarray(drawn.astype(out[name].dtype))
    for name, factor in factors.items():
        out[name] = (out[name] * factor).astype(out[name].dtype)
    return out
```

```python
import concourse.bass as bass
from concourse import mybir
from contextlib import ExitStack


def dlrm_tower(nc, ids, dense, tables, ident, w1, b1, w2, b2, w3, out):
    fp32 = mybir.dt.float32
    i32 = mybir.dt.int32
    ALU = mybir.AluOpType
    ACT = mybir.ActivationFunctionType

    P = 128
    TILES = ids.shape[0]
    NT = len(tables)
    NF = NT + 1
    D = dense.shape[2]
    NJ = NF - 1
    HALF_K = 16
    SB = 2 * P
    STEP = 4
    TURNS = TILES // STEP
    N1, N2 = w1.shape[1], w2.shape[1]
    C1, C2 = N1 // P, N2 // P
    PIECES, FILL = pair_pieces(NF)
    ZC = len(FILL)
    GROUPS = (NF + 3) // 4
    PER_TURN = STEP * GROUPS // 2
    GATHERED = 16 * NT
    MOVED = 16 * len(PIECES)

    ctx = ExitStack()
    with ctx:
        def sb(name, shape, dt=fp32):
            return ctx.enter_context(nc.sbuf_tensor(name, shape, dt))

        def sem(name):
            return ctx.enter_context(nc.semaphore(name))

        idx = [sb(f"idx{q}", [P, NT], i32) for q in range(STEP)]
        rows = [sb(f"rows{q}", [P, NF, D]) for q in range(STEP)]
        feats = [sb(f"feats{q}", [D, P, NF]) for q in range(STEP)]
        denseT = [sb(f"denseT{u}", [D, 4, 2, 32]) for u in range(2)]
        gram = [sb(f"gram{u}", [NJ, NJ, SB]) for u in range(2)]
        pairs = [sb(f"pairs{u}", [P, ZC, SB]) for u in range(2)]
        h1 = sb("h1", [P, C1, SB])
        h2 = sb("h2", [P, C2, SB])
        y = sb("y", [1, TILES * P])
        ident_sb = sb("ident_sb", [P, P])
        w1_sb = sb("w1_sb", [P, ZC + 1, N1])
        w2_sb = sb("w2_sb", [P, C1, N2])
        w3_sb = sb("w3_sb", [P, C2])
        b1_sb = sb("b1_sb", [P, C1])
        b2_sb = sb("b2_sb", [P, C2])

        psum = ctx.enter_context(nc.psum_tensor("psum", [P, 8, 512], fp32))
        TP, GP, HP = (0, 1), (2, 3), (4, 5)

        idx_in = [sem(f"idx_in{q}") for q in range(STEP)]
        dense_in = [sem(f"dense_in{q}") for q in range(STEP)]
        gathered = [sem(f"gathered{q}") for q in range(STEP)]
        ident_in = sem("ident_in")
        weights_in = sem("weights_in")
        transposed = [sem(f"transposed{b}") for b in range(2)]
        feats_out = [sem(f"feats_out{b}") for b in range(2)]
        gram_done = [sem(f"gram_done{h}") for h in range(2)]
        gram_out = [sem(f"gram_out{h}") for h in range(2)]
        pairs_in = [sem(f"pairs_in{u}") for u in range(2)]
        mlp_a = sem("mlp_a")
        mlp_b = sem("mlp_b")
        relu_act = sem("relu_act")
        relu_dve = sem("relu_dve")
        y_out = sem("y_out")
        stored = sem("stored")
        tile_begun = sem("tile_begun")

        block = ctx.enter_context(nc.Block())

        def group_bank(q, g):
            return (GROUPS * q + g) % 2

        def groups_upto(q, g, b):
            n = GROUPS * q + g + 1
            return (n + 1) // 2 if b == 0 else n // 2

        @block.sync
        def _(sp):
            def load_tile(i, q, first):
                if not first:
                    sp.wait_ge(gathered[q], GATHERED * i)
                sp.dma_start(idx[q][:, :], ids[4 * i + q, :, :]).then_inc(idx_in[q], 16)
                if not first:
                    b = group_bank(q, GROUPS - 1)
                    sp.wait_ge(transposed[b], PER_TURN * (i - 1) + groups_upto(q, GROUPS - 1, b))
                sp.dma_start(rows[q][:, 0, :], dense[4 * i + q, :, :]).then_inc(dense_in[q], 16)

            def move_pairs(s, u):
                for h in range(2):
                    sp.wait_ge(gram_out[h], 8 * (s + 1))
                for c, p0, n, j0, w in PIECES:
                    sp.dma_start(pairs[u][p0:p0 + n * w, c, :],
                                 gram[u][0:n, j0 - 1:j0 - 1 + w, :]).then_inc(pairs_in[u], 16)

            load_tile(0, 0, True)
            sp.dma_start(ident_sb[:, :], ident).then_inc(ident_in, 16)
            for q in range(1, STEP):
                load_tile(0, q, True)
            sp.dma_start(w1_sb[:, :, :], w1.rearrange("(c p) n -> p c n", p=P)).then_inc(weights_in, 16)
            sp.dma_start(w2_sb[:, :, :], w2.rearrange("(c p) n -> p c n", p=P)).then_inc(weights_in, 16)
            sp.dma_start(w3_sb[:, :], w3).then_inc(weights_in, 16)
            sp.dma_start(b1_sb[:, :], b1).then_inc(weights_in, 16)
            sp.dma_start(b2_sb[:, :], b2).then_inc(weights_in, 16)

            def turn(i, first):
                for u in range(2):
                    if not first:
                        for q in (2 * u, 2 * u + 1):
                            load_tile(i, q, False)
                    if not (first and u == 0):
                        s = 2 * i + u - 1
                        move_pairs(s, 1 - u)

            turn(0, True)
            with sp.Fori(1, TURNS) as i:
                turn(i, False)
            move_pairs(2 * TURNS - 1, 1)
            sp.wait_ge(y_out, 2 * TURNS)
            sp.dma_start(out, y[:, :]).then_inc(stored, 16)
            sp.wait_ge(stored, 16)

        @block.gpsimd
        def _(pool):
            def turn(i, first):
                for q in range(STEP):
                    pool.wait_ge(idx_in[q], 16 * (i + 1))
                    if not first:
                        b = group_bank(q, GROUPS - 1)
                        pool.wait_ge(transposed[b], PER_TURN * (i - 1) + groups_upto(q, GROUPS - 1, b))
                    pool.sem_inc(tile_begun, 1)
                    for f in range(NT):
                        pool.indirect_dma_start(
                            out=rows[q][:, f + 1, :], out_offset=None, in_=tables[f],
                            in_offset=bass.IndirectOffsetOnAxis(ap=idx[q][:, f:f + 1], axis=0),
                        ).then_inc(gathered[q], 16)

            turn(0, True)
            with pool.Fori(1, TURNS) as i:
                turn(i, False)

        def copy_feats(eng, copy, b, q, i, first):
            u, t = q // 2, q % 2
            if not first:
                eng.wait_ge(gram_done[1], 4 * i + q - 3)
            for g in range(GROUPS):
                if group_bank(q, g) != b:
                    continue
                w = min(4, NF - 4 * g)
                eng.wait_ge(transposed[b], PER_TURN * i + groups_upto(q, g, b))
                if g == 0:
                    if not first:
                        eng.wait_ge(mlp_b, 2 * (2 * i + u - 2) + 1)
                    copy(denseT[u][:, :, t, :],
                         psum[:, TP[b], 0:P].rearrange("d (s k) -> d s k", s=4))
                copy(feats[q][:, :, 4 * g:4 * g + w],
                     psum[:, TP[b], 0:w * P].rearrange("d (f n) -> d n f", f=w)).then_inc(feats_out[b], 1)

        def copy_gram(eng, copy, h, q, i, first):
            u, t = q // 2, q % 2
            eng.wait_ge(gram_done[h], 4 * i + q + 1)
            if t == 0 and not first:
                eng.wait_ge(pairs_in[u], MOVED * i)
            dst = gram[u][:, :, :].rearrange("i j (s t h k) -> i j s t h k", s=4, t=2, h=2)
            for s in range(4):
                copy(dst[:, :, s, t, h, :],
                     psum[32 * s:32 * s + NJ, GP[h], 0:HALF_K * NJ].rearrange("i (k j) -> i j k", j=NJ),
                     ).then_inc(gram_out[h], 1)

        @block.scalar
        def _(act):
            def copy(o, x):
                return nc.scalar.activation(o, x, ACT.Copy)

            def relu_layer1(s):
                act.wait_ge(mlp_a, 2 * s + 1)
                for c in range(2):
                    nc.scalar.activation(h1[:, c, :], psum[:, HP[0], c * SB:(c + 1) * SB], ACT.Relu,
                                         bias=b1_sb[:, c:c + 1]).then_inc(relu_act, 1)

            def relu_layer2(s):
                act.wait_ge(mlp_a, 2 * s + 2)
                for c in range(C2):
                    nc.scalar.activation(h2[:, c, :], psum[:, HP[0], c * SB:(c + 1) * SB], ACT.Relu,
                                         bias=b2_sb[:, c:c + 1]).then_inc(relu_act, 1)

            def copy_y(s):
                act.wait_ge(mlp_b, 2 * s + 2)
                copy(y[:, bass.ds(s * SB, SB)], psum[0:1, HP[1], 0:SB]).then_inc(y_out, 1)

            def turn(i, first):
                for u in range(2):
                    mlp = not (first and u == 0)
                    s = 2 * i + u - 1
                    copy_feats(act, copy, 0, 2 * u, i, first)
                    copy_feats(act, copy, 0, 2 * u + 1, i, first)
                    if mlp:
                        relu_layer1(s)
                    copy_gram(act, copy, 0, 2 * u, i, first)
                    if mlp:
                        relu_layer2(s)
                    copy_gram(act, copy, 0, 2 * u + 1, i, first)
                    if mlp:
                        copy_y(s)

            act.wait_ge(weights_in, 16 * 5)
            turn(0, True)
            with act.Fori(1, TURNS) as i:
                turn(i, False)
            relu_layer1(2 * TURNS - 1)
            relu_layer2(2 * TURNS - 1)
            copy_y(2 * TURNS - 1)

        @block.vector
        def _(dve):
            def copy(o, x):
                return nc.vector.tensor_copy(o, x)

            def relu_layer1(s):
                dve.wait_ge(mlp_b, 2 * s + 1)
                for c in range(2, C1):
                    nc.vector.tensor_scalar(h1[:, c, :], psum[:, HP[1], (c - 2) * SB:(c - 1) * SB],
                                            b1_sb[:, c:c + 1], 0.0, ALU.add, ALU.max).then_inc(relu_dve, 1)

            def turn(i, first):
                for u in range(2):
                    copy_feats(dve, copy, 1, 2 * u, i, first)
                    copy_feats(dve, copy, 1, 2 * u + 1, i, first)
                    if not (first and u == 0):
                        relu_layer1(2 * i + u - 1)
                    copy_gram(dve, copy, 1, 2 * u, i, first)
                    copy_gram(dve, copy, 1, 2 * u + 1, i, first)

            dve.wait_ge(weights_in, 16 * 5)
            turn(0, True)
            with dve.Fori(1, TURNS) as i:
                turn(i, False)
            relu_layer1(2 * TURNS - 1)

        @block.tensor
        def _(pe):
            def transposes(i, q, first):
                pe.wait_ge(dense_in[q], 16 * (i + 1))
                pe.wait_ge(gathered[q], GATHERED * (i + 1))
                for g in range(GROUPS):
                    b = group_bank(q, g)
                    used = groups_upto(q, g, b) - 1
                    if not (first and used == 0):
                        pe.wait_ge(feats_out[b], PER_TURN * i + used)
                    for f in range(4 * g, min(4 * g + 4, NF)):
                        last = nc.tensor.transpose(psum[:, TP[b], (f - 4 * g) * P:(f - 4 * g + 1) * P],
                                                   rows[q][:, f, :], ident_sb[:, :])
                    last.then_inc(transposed[b], 1)

            def grams(i, q, first):
                for b in range(2):
                    pe.wait_ge(feats_out[b], PER_TURN * i + groups_upto(q, GROUPS - 1, b))
                for h in range(2):
                    if not (first and q == 0):
                        pe.wait_ge(gram_out[h], 4 * (4 * i + q))
                    for k in range(HALF_K):
                        for s in range(4):
                            n = 32 * s + HALF_K * h + k
                            last = nc.tensor.matmul(psum[32 * s:32 * s + NJ, GP[h], k * NJ:(k + 1) * NJ],
                                                    feats[q][:, n, 0:NJ], feats[q][:, n, 1:NF],
                                                    start=True, stop=True)
                    last.then_inc(gram_done[h], 1)

            def layer1(s, u, uses):
                pe.wait_ge(pairs_in[u], MOVED * uses)
                for half, done in ((0, mlp_a), (1, mlp_b)):
                    if not (isinstance(s, int) and s == 0):
                        pe.wait_ge(relu_act if half == 0 else y_out, 4 * s if half == 0 else s)
                    for c in (2 * half, 2 * half + 1):
                        o = psum[:, HP[half], (c % 2) * SB:(c % 2 + 1) * SB]
                        nc.tensor.matmul(o, w1_sb[:, ZC, c * P:(c + 1) * P],
                                         denseT[u][:, :, :, :].rearrange("d s t k -> d (s t k)"),
                                         start=True, stop=False)
                        for z in range(ZC):
                            last = nc.tensor.matmul(o, w1_sb[0:FILL[z], z, c * P:(c + 1) * P],
                                                    pairs[u][0:FILL[z], z, :],
                                                    start=False, stop=(z == ZC - 1))
                    last.then_inc(done, 1)

            def layer2(s):
                pe.wait_ge(relu_act, 4 * s + 2)
                pe.wait_ge(relu_dve, 2 * s + 2)
                for m in range(C2):
                    for c in range(C1):
                        last = nc.tensor.matmul(psum[:, HP[0], m * SB:(m + 1) * SB],
                                                w2_sb[:, c, m * P:(m + 1) * P], h1[:, c, :],
                                                start=(c == 0), stop=(c == C1 - 1))
                last.then_inc(mlp_a, 1)

            def layer3(s):
                pe.wait_ge(relu_act, 4 * s + 4)
                for m in range(C2):
                    last = nc.tensor.matmul(psum[0:1, HP[1], 0:SB], w3_sb[:, m:m + 1], h2[:, m, :],
                                            start=(m == 0), stop=(m == C2 - 1))
                last.then_inc(mlp_b, 1)

            def turn(i, first):
                for u in range(2):
                    mlp = not (first and u == 0)
                    s = 2 * i + u - 1
                    transposes(i, 2 * u, first)
                    transposes(i, 2 * u + 1, first)
                    if mlp:
                        layer1(s, 1 - u, i + u)
                    grams(i, 2 * u, first)
                    if mlp:
                        layer2(s)
                    grams(i, 2 * u + 1, first)
                    if mlp:
                        layer3(s)

            pe.wait_ge(ident_in, 16)
            pe.wait_ge(weights_in, 16 * 5)
            turn(0, True)
            with pe.Fori(1, TURNS) as i:
                turn(i, False)
            layer1(2 * TURNS - 1, 1, TURNS)
            layer2(2 * TURNS - 1)
            layer3(2 * TURNS - 1)


def pair_pieces(nf):
    sizes, top = [], nf - 1
    while top > 0:
        w = min(3, top)
        sizes.append((top, top - w + 1, w))
        top -= w
    fill, pieces = [], []
    for n, j0, w in sizes:
        c = next((c for c, x in enumerate(fill) if x + n * w <= 128), None)
        if c is None:
            c = len(fill)
            fill.append(0)
        pieces.append((c, fill[c], n, j0, w))
        fill[c] += n * w
    return pieces, fill


def kernel(**inputs):
    import numpy as np
    import concourse.bacc as bacc
    from concourse.bass_utils import run_bass_kernel_spmd

    ids = np.asarray(inputs["ids"])
    dense = np.asarray(inputs["r_dense_features"])
    w1 = np.asarray(inputs["W_top1"])
    batch, nt = ids.shape
    nf, d = nt + 1, dense.shape[1]

    def by_tile(a):
        return a.reshape(batch // 256, 4, 2, 32, -1).transpose(0, 2, 1, 3, 4).reshape(batch // 128, 128, -1)

    pieces, fill = pair_pieces(nf)
    rows = np.full((len(fill) + 1, 128), -1)
    row_of = {(i, j): n for n, (i, j) in enumerate(zip(*np.triu_indices(nf, 1)))}
    for c, p0, n, j0, w in pieces:
        for i in range(n):
            for jj in range(w):
                if i < j0 + jj:
                    rows[c, p0 + w * i + jj] = row_of[i, j0 + jj]
    rows[-1, :d] = len(row_of) + np.arange(d)
    padded = np.concatenate([w1, np.zeros((1, w1.shape[1]), w1.dtype)])
    arrays = {
        "ids": by_tile(ids),
        "dense": by_tile(dense),
        "ident": np.eye(128, dtype=np.float32),
        "w1": padded[rows.ravel()],
        "b1": np.asarray(inputs["b_top1"]).reshape(-1, 128).T,
        "w2": np.asarray(inputs["W_top2"]),
        "b2": np.asarray(inputs["b_top2"]).reshape(-1, 128).T,
        "w3": np.asarray(inputs["W_top3"]).reshape(-1, 128).T,
    }
    for f in range(nt):
        arrays[f"table{f}"] = np.asarray(inputs[f"tbl_{f}"])
    arrays = {k: np.ascontiguousarray(v) for k, v in arrays.items()}

    nc = bacc.Bacc("TRN2", target_bir_lowering=False, num_devices=1)
    ap = {k: nc.dram_tensor(k, v.shape, mybir.dt.from_np(v.dtype), kind="ExternalInput").ap()
          for k, v in arrays.items()}
    out = nc.dram_tensor("out", (1, batch), mybir.dt.float32, kind="ExternalOutput").ap()
    dlrm_tower(nc, ap["ids"], ap["dense"], [ap[f"table{f}"] for f in range(nt)], ap["ident"],
               ap["w1"], ap["b1"], ap["w2"], ap["b2"], ap["w3"], out)
    r = run_bass_kernel_spmd(nc, [arrays], core_ids=[0])
    return r.results[0]["out"].reshape(batch, 1)
```

```python
import concourse.bass as bass
from concourse import mybir
from contextlib import ExitStack


NUM_HOT = 8


def dlrm_tower(nc, ids, dense, tables, ident, hot_ids, hot_tables, hot_rows, pick, w1, b1, w2, b2, w3, out):
    fp32 = mybir.dt.float32
    fp32r = mybir.dt.float32r
    fp16 = mybir.dt.float16
    i32 = mybir.dt.int32
    ALU = mybir.AluOpType
    ACT = mybir.ActivationFunctionType

    P = 128
    TURNS = ids.shape[0] // 2
    NC = len(tables)
    NH = len(hot_tables)
    NR = NC + 1
    NF = NR + NH
    D = dense.shape[2]
    NJ = NF - 1
    HALF_K = 16
    SB = 2 * P
    HP_ROWS, HC = hot_rows.shape
    SLOTS = 4
    N1, N2 = w1.shape[1], w2.shape[1]
    C1, C2 = N1 // P, N2 // P
    PIECES, FILL = pair_pieces(NF)
    ZC = len(FILL)
    GROUPS = (NR + 3) // 4
    FRONT = NH // 2 + GROUPS
    GATHERED = 16 * NC
    MOVED = 16 * len(PIECES)
    RELUS = C1 + C2
    assert NH % SLOTS == 0 and C1 == 4 and C2 == 2 and NR + NH == 27

    ctx = ExitStack()
    with ctx:
        def sb(name, shape, dt=fp32):
            return ctx.enter_context(nc.sbuf_tensor(name, shape, dt))

        def sem(name):
            return ctx.enter_context(nc.semaphore(name))

        idx = [sb(f"idx{t}", [P, NC], i32) for t in range(2)]
        rows = [sb(f"rows{t}", [P, NR, D]) for t in range(2)]
        feats = sb("feats", [D, 2, P, NF])
        denseT = sb("denseT", [D, 4, 2, 32])
        gram = sb("gram", [P, NJ * SB])
        pairs = sb("pairs", [P, ZC, SB])
        h1 = sb("h1", [P, C1, SB])
        h2 = sb("h2", [P, C2, SB])
        y = sb("y", [1, TURNS * SB])
        ident_sb = sb("ident_sb", [P, P])
        w1_sb = sb("w1_sb", [P, ZC + 1, N1])
        w2_sb = sb("w2_sb", [P, C1, N2])
        w3_sb = sb("w3_sb", [P, C2])
        b1_sb = sb("b1_sb", [P, C1])
        b2_sb = sb("b2_sb", [P, C2])
        hot_hi = sb("hot_hi", [P, NH, HC, D], fp32r)
        hot_lo = sb("hot_lo", [P, NH, HC, D], fp32r)
        onehot = [sb(f"onehot{n}", [P, HC, SB], fp32r) for n in range(SLOTS)]
        hot_rows_sb = sb("hot_rows_sb", [P, HC])
        hot_ids_sb = sb("hot_ids_sb", [NH, TURNS * SB], fp16)
        pick_sb = sb("pick_sb", [NH, NH, P], fp16)

        raw = [gram[0:HP_ROWS, n * HC * D:(n + 1) * HC * D] for n in range(SLOTS)]
        raw_ids = gram[0:NH, SLOTS * HC * D:SLOTS * HC * D + TURNS * SB].bitcast(i32)

        psum = ctx.enter_context(nc.psum_tensor("psum", [P, 8, 512], fp32))
        FP, GP, HP, IP = (0, 1), (2, 3), (4, 5), (6, 7)

        idx_in = [sem(f"idx_in{t}") for t in range(2)]
        dense_in = [sem(f"dense_in{t}") for t in range(2)]
        gathered = [sem(f"gathered{t}") for t in range(2)]
        raw_in = [sem(f"raw_in{n}") for n in range(SLOTS)]
        ids_in = sem("ids_in")
        consts_in = sem("consts_in")
        weights_in = sem("weights_in")
        hot_split = sem("hot_split")
        ids_cast = sem("ids_cast")
        spread = sem("spread")
        compared = sem("compared")
        front = [sem(f"front{b}") for b in range(2)]
        front_out = [sem(f"front_out{b}") for b in range(2)]
        gram_done = [sem(f"gram_done{h}") for h in range(2)]
        gram_out = [sem(f"gram_out{h}") for h in range(2)]
        pairs_in = sem("pairs_in")
        mlp_a = sem("mlp_a")
        mlp_b = sem("mlp_b")
        relu_out = sem("relu_out")
        y_out = sem("y_out")
        stored = sem("stored")
        tile_begun = sem("tile_begun")

        block = ctx.enter_context(nc.Block())

        def front_use(t, g):
            n = NH + GROUPS * t + g
            return n % 2, n // 2 + 1

        def wait_transposed(eng, s, t):
            b, n = front_use(t, GROUPS - 1)
            eng.wait_ge(front[b], FRONT * s + n)

        @block.sync
        def _(sp):
            def load_tiles(s):
                for t in range(2):
                    sp.wait_ge(gathered[t], GATHERED * s)
                    sp.dma_start(idx[t][:, :], ids[2 * s + t, :, :]).then_inc(idx_in[t], 16)
                for t in range(2):
                    wait_transposed(sp, s - 1, t)
                    sp.dma_start(rows[t][:, 0, :], dense[2 * s + t, :, :]).then_inc(dense_in[t], 16)

            def move_pairs(s):
                for h in range(2):
                    sp.wait_ge(gram_out[h], 8 * (s + 1))
                for c, p0, n, j0, w in PIECES:
                    sp.dma_start(pairs[p0:p0 + n * w, c, :],
                                 gram[0:n, (j0 - 1) * SB:(j0 - 1 + w) * SB].rearrange(
                                     "i (j b) -> i j b", j=w)).then_inc(pairs_in, 16)

            for t in range(2):
                sp.dma_start(idx[t][:, :], ids[t, :, :]).then_inc(idx_in[t], 16)
            sp.dma_start(raw_ids, hot_ids).then_inc(ids_in, 16)
            sp.dma_start(pick_sb[:, :, :], pick).then_inc(consts_in, 16)
            sp.dma_start(hot_rows_sb[0:HP_ROWS, :], hot_rows).then_inc(consts_in, 16)
            sp.dma_start(ident_sb[:, :], ident).then_inc(consts_in, 16)
            for f in range(NH):
                if f >= SLOTS:
                    sp.wait_ge(hot_split, 2 * (f - SLOTS + 1))
                sp.dma_start(raw[f % SLOTS], hot_tables[f].rearrange("(p c) d -> p (c d)", c=HC)
                             ).then_inc(raw_in[f % SLOTS], 16)
                if f == SLOTS - 1:
                    for t in range(2):
                        sp.dma_start(rows[t][:, 0, :], dense[t, :, :]).then_inc(dense_in[t], 16)
                    sp.dma_start(w1_sb[:, :, :], w1.rearrange("(c p) n -> p c n", p=P)).then_inc(weights_in, 16)
                    sp.dma_start(w2_sb[:, :, :], w2.rearrange("(c p) n -> p c n", p=P)).then_inc(weights_in, 16)
                    sp.dma_start(w3_sb[:, :], w3).then_inc(weights_in, 16)
                    sp.dma_start(b1_sb[:, :], b1).then_inc(weights_in, 16)
                    sp.dma_start(b2_sb[:, :], b2).then_inc(weights_in, 16)

            with sp.Fori(1, TURNS) as s:
                load_tiles(s)
                move_pairs(s - 1)
            move_pairs(TURNS - 1)
            sp.wait_ge(y_out, TURNS)
            sp.dma_start(out, y[:, :]).then_inc(stored, 16)
            sp.wait_ge(stored, 16)

        @block.gpsimd
        def _(pool):
            def turn(s, first):
                for t in range(2):
                    pool.wait_ge(idx_in[t], 16 * (s + 1))
                    if not first:
                        wait_transposed(pool, s - 1, t)
                    pool.sem_inc(tile_begun, 1)
                    for f in range(NC):
                        pool.indirect_dma_start(
                            out=rows[t][:, f + 1, :], out_offset=None, in_=tables[f],
                            in_offset=bass.IndirectOffsetOnAxis(ap=idx[t][:, f:f + 1], axis=0),
                        ).then_inc(gathered[t], 16)

            turn(0, True)
            with pool.Fori(1, TURNS) as s:
                turn(s, False)

        @block.vector
        def _(dve):
            def compare(s, f, first):
                dve.wait_ge(spread, NH * s + f - f % 2 + 2)
                if f >= SLOTS:
                    dve.wait_ge(front[f % 2], FRONT * s + (f - SLOTS) // 2 + 1)
                elif not first:
                    dve.wait_ge(front[f % 2], FRONT * (s - 1) + (f + NH - SLOTS) // 2 + 1)
                ids_b = psum[0:HP_ROWS, IP[f // 2 % 2], (f % 2) * SB:(f % 2 + 1) * SB]
                nc.vector.tensor_tensor(
                    onehot[f % SLOTS][0:HP_ROWS, :, :],
                    ids_b.rearrange("p (o b) -> p o b", o=1).to_broadcast([HP_ROWS, HC, SB]),
                    hot_rows_sb[0:HP_ROWS, :].rearrange("p (c o) -> p c o", o=1).to_broadcast(
                        [HP_ROWS, HC, SB]),
                    ALU.is_equal).then_inc(compared, 1)

            def split(f):
                dve.wait_ge(raw_in[f % SLOTS], 16 * (f // SLOTS + 1))
                hi, lo = (x[0:HP_ROWS, f, :, :].rearrange("p c d -> p (c d)") for x in (hot_hi, hot_lo))
                nc.vector.tensor_copy(hi, raw[f % SLOTS]).then_inc(hot_split, 1)
                dve.wait_ge(hot_split, 2 * f + 1)
                nc.vector.tensor_tensor(lo, raw[f % SLOTS], hi.bitcast(fp32), ALU.subtract).then_inc(hot_split, 1)

            dve.wait_ge(ids_in, 16)
            nc.vector.tensor_copy(hot_ids_sb[:, :], raw_ids).then_inc(ids_cast, 1)
            dve.wait_ge(consts_in, 16 * 3)
            for f in range(NH):
                split(f)
                if f >= SLOTS:
                    compare(0, f - SLOTS, True)
            for f in range(SLOTS, NH):
                compare(0, f, True)
            with dve.Fori(1, TURNS) as s:
                for f in range(NH):
                    compare(s, f, False)

        @block.scalar
        def _(act):
            def copy(o, x):
                return nc.scalar.activation(o, x, ACT.Copy)

            def copy_hot(s, f):
                act.wait_ge(front[f % 2], FRONT * s + f // 2 + 1)
                copy(feats[:, :, :, NR + f].rearrange("d t n -> d (t n)"),
                     psum[:, FP[f % 2], 0:SB]).then_inc(front_out[f % 2], 1)

            def copy_rows(s, t):
                for g in range(GROUPS):
                    w = min(4, NR - 4 * g)
                    b, n = front_use(t, g)
                    act.wait_ge(front[b], FRONT * s + n)
                    if g == 0:
                        copy(denseT[:, :, t, :], psum[:, FP[b], 0:P].rearrange("d (s k) -> d s k", s=4))
                    copy(feats[:, t, :, 4 * g:4 * g + w],
                         psum[:, FP[b], 0:w * P].rearrange("d (f n) -> d n f", f=w)).then_inc(front_out[b], 1)

            def copy_gram(s, t, first):
                dst = gram[0:NJ, :].rearrange("i (j s t h k) -> i j s t h k", j=NJ, s=4, t=2, h=2)
                if t == 0 and not first:
                    act.wait_ge(pairs_in, MOVED * s)
                for h in range(2):
                    act.wait_ge(gram_done[h], 2 * s + t + 1)
                    for q in range(4):
                        copy(dst[:, :, q, t, h, :],
                             psum[32 * q:32 * q + NJ, GP[h], 0:HALF_K * NJ].rearrange(
                                 "i (k j) -> i j k", j=NJ)).then_inc(gram_out[h], 1)

            def relu(dst, bias, bank, chunks):
                for n, c in enumerate(chunks):
                    nc.scalar.activation(dst[:, c, :], psum[:, bank, n * SB:(n + 1) * SB], ACT.Relu,
                                         bias=bias[:, c:c + 1]).then_inc(relu_out, 1)

            def layer1a(s):
                act.wait_ge(mlp_a, 2 * s + 1)
                relu(h1, b1_sb, HP[0], (0, 1))

            def layer1b(s):
                act.wait_ge(mlp_b, 2 * s + 1)
                relu(h1, b1_sb, HP[1], (2, 3))

            def layer2(s):
                act.wait_ge(mlp_a, 2 * s + 2)
                relu(h2, b2_sb, HP[0], (0, 1))

            def layer3(s):
                act.wait_ge(mlp_b, 2 * s + 2)
                copy(y[:, bass.ds(s * SB, SB)], psum[0:1, HP[1], 0:SB]).then_inc(y_out, 1)

            def turn(s, first):
                for f in range(0, 4):
                    copy_hot(s, f)
                if not first:
                    layer1a(s - 1)
                for f in range(4, 6):
                    copy_hot(s, f)
                if not first:
                    layer1b(s - 1)
                for f in range(6, NH):
                    copy_hot(s, f)
                if not first:
                    layer2(s - 1)
                copy_rows(s, 0)
                if not first:
                    layer3(s - 1)
                copy_rows(s, 1)
                copy_gram(s, 0, first)
                copy_gram(s, 1, first)

            act.wait_ge(weights_in, 16 * 5)
            turn(0, True)
            with act.Fori(1, TURNS) as s:
                turn(s, False)
            for layer in (layer1a, layer1b, layer2, layer3):
                layer(TURNS - 1)

        @block.tensor
        def _(pe):
            def spread_ids(s, f):
                nc.tensor.matmul(psum[0:HP_ROWS, IP[f // 2 % 2], (f % 2) * SB:(f % 2 + 1) * SB],
                                 pick_sb[:, f, 0:HP_ROWS], hot_ids_sb[:, bass.ds(s * SB, SB)],
                                 start=True, stop=True).then_inc(spread, 1)

            def hot(s, f, first, last_turn):
                if f % 2 == 0:
                    pe.wait_ge(compared, NH * s + f + 2)
                if first:
                    pe.wait_ge(hot_split, 2 * f + 2)
                b, n = f % 2, f // 2
                if not (first and n == 0):
                    pe.wait_ge(front_out[b], FRONT * s + n)
                for part in (hot_hi, hot_lo):
                    for c in range(HC):
                        last = nc.tensor.matmul(psum[:, FP[b], 0:SB], part[0:HP_ROWS, f, c, :],
                                                onehot[f % SLOTS][0:HP_ROWS, c, :],
                                                start=(part is hot_hi and c == 0),
                                                stop=(part is hot_lo and c == HC - 1))
                last.then_inc(front[b], 1)
                if f % 2 == 0:
                    for n in (f + 4, f + 5):
                        if n < NH:
                            spread_ids(s, n)
                        elif not last_turn:
                            spread_ids(s + 1, n - NH)

            def transposes(s, t):
                pe.wait_ge(dense_in[t], 16 * (s + 1))
                pe.wait_ge(gathered[t], GATHERED * (s + 1))
                for g in range(GROUPS):
                    b, n = front_use(t, g)
                    pe.wait_ge(front_out[b], FRONT * s + n - 1)
                    for f in range(4 * g, min(4 * g + 4, NR)):
                        last = nc.tensor.transpose(psum[:, FP[b], (f - 4 * g) * P:(f - 4 * g + 1) * P],
                                                   rows[t][:, f, :], ident_sb[:, :])
                    last.then_inc(front[b], 1)

            def grams(s, t, first):
                for g in (GROUPS - 2, GROUPS - 1):
                    b, n = front_use(t, g)
                    pe.wait_ge(front_out[b], FRONT * s + n)
                for h in range(2):
                    if not (first and t == 0):
                        pe.wait_ge(gram_out[h], 4 * (2 * s + t))
                    for k in range(HALF_K):
                        for q in range(4):
                            n = 32 * q + HALF_K * h + k
                            last = nc.tensor.matmul(psum[32 * q:32 * q + NJ, GP[h], k * NJ:(k + 1) * NJ],
                                                    feats[:, t, n, 0:NJ], feats[:, t, n, 1:NF],
                                                    start=True, stop=True)
                    last.then_inc(gram_done[h], 1)

            def layer1(half, done):
                for c in (2 * half, 2 * half + 1):
                    o = psum[:, HP[half], (c % 2) * SB:(c % 2 + 1) * SB]
                    nc.tensor.matmul(o, w1_sb[:, ZC, c * P:(c + 1) * P],
                                     denseT[:, :, :, :].rearrange("d s t k -> d (s t k)"),
                                     start=True, stop=False)
                    for z in range(ZC):
                        last = nc.tensor.matmul(o, w1_sb[0:FILL[z], z, c * P:(c + 1) * P],
                                                pairs[0:FILL[z], z, :], start=False, stop=(z == ZC - 1))
                last.then_inc(done, 1)

            def layer1a(s):
                pe.wait_ge(pairs_in, MOVED * (s + 1))
                layer1(0, mlp_a)

            def layer1b(s):
                layer1(1, mlp_b)

            def layer2(s):
                pe.wait_ge(relu_out, RELUS * s + C1)
                for m in range(C2):
                    for c in range(C1):
                        last = nc.tensor.matmul(psum[:, HP[0], m * SB:(m + 1) * SB],
                                                w2_sb[:, c, m * P:(m + 1) * P], h1[:, c, :],
                                                start=(c == 0), stop=(c == C1 - 1))
                last.then_inc(mlp_a, 1)

            def layer3(s):
                pe.wait_ge(relu_out, RELUS * (s + 1))
                for m in range(C2):
                    last = nc.tensor.matmul(psum[0:1, HP[1], 0:SB], w3_sb[:, m:m + 1], h2[:, m, :],
                                            start=(m == 0), stop=(m == C2 - 1))
                last.then_inc(mlp_b, 1)

            def turn(s, first, last_turn, prev_used):
                for f in range(0, 4):
                    hot(s, f, first, last_turn)
                if not first:
                    if prev_used:
                        pe.wait_ge(relu_out, RELUS * (s - 1))
                    layer1a(s - 1)
                for f in range(4, 6):
                    hot(s, f, first, last_turn)
                if not first:
                    if prev_used:
                        pe.wait_ge(y_out, s - 1)
                    layer1b(s - 1)
                for f in range(6, NH):
                    hot(s, f, first, last_turn)
                if not first:
                    layer2(s - 1)
                transposes(s, 0)
                if not first:
                    layer3(s - 1)
                transposes(s, 1)
                grams(s, 0, first)
                grams(s, 1, first)

            pe.wait_ge(consts_in, 16 * 3)
            pe.wait_ge(ids_cast, 1)
            for f in range(4):
                spread_ids(0, f)
            turn(0, True, False, False)
            pe.wait_ge(weights_in, 16 * 5)
            with pe.Fori(1, TURNS - 1) as s:
                turn(s, False, False, True)
            turn(TURNS - 1, False, True, True)
            pe.wait_ge(relu_out, RELUS * (TURNS - 1))
            layer1a(TURNS - 1)
            pe.wait_ge(y_out, TURNS - 1)
            layer1b(TURNS - 1)
            layer2(TURNS - 1)
            layer3(TURNS - 1)


def pair_pieces(nf):
    sizes, top = [], nf - 1
    while top > 0:
        w = min(3, top)
        sizes.append((top, top - w + 1, w))
        top -= w
    fill, pieces = [], []
    for n, j0, w in sizes:
        c = next((c for c, x in enumerate(fill) if x + n * w <= 128), None)
        if c is None:
            c = len(fill)
            fill.append(0)
        pieces.append((c, fill[c], n, j0, w))
        fill[c] += n * w
    return pieces, fill


def kernel(**inputs):
    import numpy as np
    import concourse.bacc as bacc
    from concourse.bass_utils import run_bass_kernel_spmd

    ids = np.asarray(inputs["ids"])
    dense = np.asarray(inputs["r_dense_features"])
    w1 = np.asarray(inputs["W_top1"])
    tables = [np.asarray(inputs[f"tbl_{f}"]) for f in range(ids.shape[1])]
    batch, d = dense.shape
    nf = len(tables) + 1

    hot = [f for f, x in enumerate(tables) if x.shape[0] == 1000][:NUM_HOT]
    cold = [f for f in range(len(tables)) if f not in hot]
    order = [0] + [f + 1 for f in cold + hot]

    def by_tile(a):
        return a.reshape(batch // 256, 4, 2, 32, -1).transpose(0, 2, 1, 3, 4).reshape(batch // 128, 128, -1)

    pieces, fill = pair_pieces(nf)
    rows = np.full((len(fill) + 1, 128), -1)
    row_of = {(i, j): n for n, (i, j) in enumerate(zip(*np.triu_indices(nf, 1)))}
    for c, p0, n, j0, w in pieces:
        for i in range(n):
            for j in range(j0, j0 + w):
                if i < j:
                    rows[c, p0 + w * i + j - j0] = row_of[tuple(sorted((order[i], order[j])))]
    rows[-1, :d] = len(row_of) + np.arange(d)
    padded = np.concatenate([w1, np.zeros((1, w1.shape[1]), w1.dtype)])
    by_tiles = by_tile(ids)
    arrays = {
        "ids": by_tiles[:, :, cold],
        "dense": by_tile(dense),
        "ident": np.eye(128, dtype=np.float32),
        "hot_ids": by_tiles[:, :, hot].transpose(2, 0, 1).reshape(len(hot), batch),
        "hot_rows": np.arange(1000, dtype=np.float32).reshape(125, 8),
        "pick": np.repeat(np.eye(len(hot), dtype=np.float16)[:, :, None], 128, axis=2),
        "w1": padded[rows.ravel()],
        "b1": np.asarray(inputs["b_top1"]).reshape(-1, 128).T,
        "w2": np.asarray(inputs["W_top2"]),
        "b2": np.asarray(inputs["b_top2"]).reshape(-1, 128).T,
        "w3": np.asarray(inputs["W_top3"]).reshape(-1, 128).T,
    }
    for f, x in enumerate(tables):
        arrays[f"table{f}"] = x
    arrays = {k: np.ascontiguousarray(v) for k, v in arrays.items()}

    nc = bacc.Bacc("TRN2", target_bir_lowering=False, num_devices=1)
    ap = {k: nc.dram_tensor(k, v.shape, mybir.dt.from_np(v.dtype), kind="ExternalInput").ap()
          for k, v in arrays.items()}
    out = nc.dram_tensor("out", (1, batch), mybir.dt.float32, kind="ExternalOutput").ap()
    dlrm_tower(nc, ap["ids"], ap["dense"], [ap[f"table{f}"] for f in cold], ap["ident"], ap["hot_ids"],
               [ap[f"table{f}"] for f in hot], ap["hot_rows"], ap["pick"],
               ap["w1"], ap["b1"], ap["w2"], ap["b2"], ap["w3"], out)
    r = run_bass_kernel_spmd(nc, [arrays], core_ids=[0])
    return r.results[0]["out"].reshape(batch, 1)
```

```python
import concourse.bass as bass
from concourse import mybir
from contextlib import ExitStack


NUM_HOT = 8


def dlrm_tower(nc, ids, dense, tables, ident, hot_ids, hot_tables, hot_rows, pick, w1, b1, w2, b2, w3, out):
    fp32 = mybir.dt.float32
    fp32r = mybir.dt.float32r
    fp16 = mybir.dt.float16
    i32 = mybir.dt.int32
    ALU = mybir.AluOpType
    ACT = mybir.ActivationFunctionType

    P = 128
    TURNS = ids.shape[0] // 2
    NC = len(tables)
    NH = len(hot_tables)
    NR = NC + 1
    NF = NR + NH
    D = dense.shape[2]
    NJ = NF - 1
    HALF_K = 16
    SB = 2 * P
    HP_ROWS, HC = hot_rows.shape
    SLOTS = 4
    N1, N2 = w1.shape[1], w2.shape[1]
    C1, C2 = N1 // P, N2 // P
    PIECES, FILL = pair_pieces(NF)
    ZC = len(FILL)
    GROUPS = (NR + 3) // 4
    GATHERED = 16 * NC
    MOVED = 16 * len(PIECES)
    RELUS = C1 + C2
    assert NH == 8 and SLOTS == 4 and GROUPS == 5 and C1 == 4 and C2 == 2 and NR + NH == 27

    FRONTS = [("hot", 0), ("hot", 1), ("hot", 2), ("rows", 0, 0), ("hot", 3), ("rows", 0, 1), ("hot", 4),
              ("rows", 0, 2), ("hot", 5), ("rows", 0, 3), ("hot", 6), ("rows", 0, 4), ("hot", 7)]
    TILE1 = [("rows", 1, g) for g in range(GROUPS)]
    FRONT = (len(FRONTS) + GROUPS) // 2
    STEPS = (FRONTS + TILE1[:2] + [("gram", 0, 0)] + TILE1[2:4] + [("gram", 0, 1)] + TILE1[4:]
             + [("layer", "1a"), ("layer", "1b"), ("dense",), ("gram", 1, 0), ("layer", "2"),
                ("gram", 1, 1), ("layer", "3")])
    LAST_STEPS = (FRONTS + [("gram", 0, 0), ("gram", 0, 1)] + TILE1
                  + [("gram", 1, 0), ("gram", 1, 1), ("layer", "1a"), ("layer", "1b"), ("dense",),
                     ("layer", "2"), ("layer", "3")])

    ctx = ExitStack()
    with ctx:
        def sb(name, shape, dt=fp32):
            return ctx.enter_context(nc.sbuf_tensor(name, shape, dt))

        def sem(name):
            return ctx.enter_context(nc.semaphore(name))

        idx = [sb(f"idx{t}", [P, NC], i32) for t in range(2)]
        rows = [sb(f"rows{t}", [P, NR, D]) for t in range(2)]
        feats = sb("feats", [D, 2, P, NF])
        dense_hi = sb("dense_hi", [D, 4, 2, 32], fp32r)
        dense_lo = sb("dense_lo", [D, 4, 2, 32], fp32r)
        gram = sb("gram", [P, NJ * SB])
        pairs = sb("pairs", [P, ZC, SB])
        pairs_hi = sb("pairs_hi", [P, ZC, SB], fp32r)
        pairs_lo = sb("pairs_lo", [P, ZC, SB], fp32r)
        h1 = sb("h1", [P, C1, SB])
        h2 = h1[:, 0:C2, :]
        ident_sb = sb("ident_sb", [P, P])
        w1_hi = sb("w1_hi", [P, ZC + 1, N1], fp32r)
        w1_lo = sb("w1_lo", [P, ZC + 1, N1], fp32r)
        w2_sb = sb("w2_sb", [P, C1, N2])
        w3_sb = sb("w3_sb", [P, C2])
        b1_sb = sb("b1_sb", [P, C1])
        b2_sb = sb("b2_sb", [P, C2])
        hot_hi = sb("hot_hi", [P, NH, HC, D], fp32r)
        hot_lo = sb("hot_lo", [P, NH, HC, D], fp32r)
        onehot = [sb(f"onehot{n}", [P, HC, SB], fp32r) for n in range(SLOTS)]
        hot_rows_sb = sb("hot_rows_sb", [P, HC])
        hot_ids_sb = sb("hot_ids_sb", [NH, TURNS * SB], fp16)
        pick_sb = sb("pick_sb", [NH, NH], fp16)
        y = gram[64:65, 0:TURNS * SB]

        raw = [gram[0:HP_ROWS, n * HC * D:(n + 1) * HC * D] for n in range(SLOTS)]
        raw_w1 = h1[:, :, :].rearrange("p c n -> p (c n)")
        raw_ids = gram[0:NH, SLOTS * HC * D:SLOTS * HC * D + TURNS * SB].bitcast(i32)

        psum = ctx.enter_context(nc.psum_tensor("psum", [P, 8, 512], fp32))
        FP, GP, HP, IP = (0, 1), (2, 3), (4, 5), (6, 7)

        idx_in = [sem(f"idx_in{t}") for t in range(2)]
        dense_in = [sem(f"dense_in{t}") for t in range(2)]
        gathered = [sem(f"gathered{t}") for t in range(2)]
        raw_in = [sem(f"raw_in{n}") for n in range(SLOTS)]
        ids_in = sem("ids_in")
        consts_in = sem("consts_in")
        weights_in = sem("weights_in")
        raw_w1_in = sem("raw_w1_in")
        w1_rounded = sem("w1_rounded")
        w1_split = sem("w1_split")
        pairs_rounded = sem("pairs_rounded")
        pairs_split = sem("pairs_split")
        dense_rounded = sem("dense_rounded")
        hot_rounded = sem("hot_rounded")
        hot_split = sem("hot_split")
        ids_cast = sem("ids_cast")
        spread = sem("spread")
        compared = sem("compared")
        front = [sem(f"front{b}") for b in range(2)]
        front_out = [sem(f"front_out{b}") for b in range(2)]
        gram_done = [sem(f"gram_done{h}") for h in range(2)]
        gram_out = [sem(f"gram_out{h}") for h in range(2)]
        pairs_in = sem("pairs_in")
        mlp_a = sem("mlp_a")
        mlp_b = sem("mlp_b")
        relu_out = sem("relu_out")
        dense_out = sem("dense_out")
        y_out = sem("y_out")
        stored = sem("stored")
        tile_begun = sem("tile_begun")

        block = ctx.enter_context(nc.Block())

        def front_use(*use):
            n = (FRONTS + TILE1).index(use)
            return n % 2, n // 2 + 1

        def wait_front(eng, sems, s, *use):
            b, n = front_use(*use)
            eng.wait_ge(sems[b], FRONT * s + n)

        def wait_transposed(eng, s, t):
            wait_front(eng, front, s, "rows", t, GROUPS - 1)

        def copy_gram(eng, copy, h, s, t, first):
            dst = gram[0:NJ, :].rearrange("i (j s t h k) -> i j s t h k", j=NJ, s=4, t=2, h=2)
            if t == 0 and not first:
                eng.wait_ge(pairs_in, MOVED * s)
            eng.wait_ge(gram_done[h], 2 * s + t + 1)
            for q in range(4):
                copy(dst[:, :, q, t, h, :],
                     psum[32 * q:32 * q + NJ, GP[h], 0:HALF_K * NJ].rearrange(
                         "i (k j) -> i j k", j=NJ)).then_inc(gram_out[h], 1)

        W1_HALVES = ((0, 2), (2, 4))

        @block.sync
        def _(sp):
            def load_ids(s):
                for t in range(2):
                    sp.wait_ge(gathered[t], GATHERED * s)
                    sp.dma_start(idx[t][:, :], ids[2 * s + t, :, :]).then_inc(idx_in[t], 16)

            def load_dense(s):
                for t in range(2):
                    wait_transposed(sp, s - 1, t)
                    sp.dma_start(rows[t][:, 0, :], dense[2 * s + t, :, :]).then_inc(dense_in[t], 16)

            def move_pairs(s):
                for h in range(2):
                    sp.wait_ge(gram_out[h], 8 * (s + 1))
                for c, p0, n, j0, w in PIECES:
                    sp.dma_start(pairs[p0:p0 + n * w, c, :],
                                 gram[0:n, (j0 - 1) * SB:(j0 - 1 + w) * SB].rearrange(
                                     "i (j b) -> i j b", j=w)).then_inc(pairs_in, 16)

            def load_w1(half):
                a, b = W1_HALVES[half]
                sp.dma_start(raw_w1.rearrange("p (c n) -> p c n", n=N1),
                             w1.rearrange("(c p) n -> p c n", p=P)[:, a:b, :]).then_inc(raw_w1_in, 16)

            for t in range(2):
                sp.dma_start(idx[t][:, :], ids[t, :, :]).then_inc(idx_in[t], 16)
            sp.dma_start(raw_ids, hot_ids).then_inc(ids_in, 16)
            sp.dma_start(pick_sb[:, :], pick).then_inc(consts_in, 16)
            sp.dma_start(hot_rows_sb[0:HP_ROWS, :], hot_rows).then_inc(consts_in, 16)
            sp.dma_start(ident_sb[:, :], ident).then_inc(consts_in, 16)
            for f in range(NH):
                if f >= SLOTS:
                    sp.wait_ge(hot_split, f - SLOTS + 1)
                sp.dma_start(raw[f % SLOTS], hot_tables[f].rearrange("(p c) d -> p (c d)", c=HC)
                             ).then_inc(raw_in[f % SLOTS], 16)
                if f == SLOTS - 1:
                    for t in range(2):
                        sp.dma_start(rows[t][:, 0, :], dense[t, :, :]).then_inc(dense_in[t], 16)
                    load_w1(0)
                    sp.dma_start(w2_sb[:, :, :], w2.rearrange("(c p) n -> p c n", p=P)).then_inc(weights_in, 16)
                    sp.dma_start(w3_sb[:, :], w3).then_inc(weights_in, 16)
                    sp.dma_start(b1_sb[:, :], b1).then_inc(weights_in, 16)
                    sp.dma_start(b2_sb[:, :], b2).then_inc(weights_in, 16)

            load_ids(1)
            sp.wait_ge(w1_split, 1)
            load_w1(1)
            load_dense(1)
            move_pairs(0)
            with sp.Fori(2, TURNS) as s:
                load_ids(s)
                load_dense(s)
                move_pairs(s - 1)
            move_pairs(TURNS - 1)
            sp.wait_ge(y_out, TURNS)
            sp.dma_start(out, y).then_inc(stored, 16)
            sp.wait_ge(stored, 16)

        @block.gpsimd
        def _(pool):
            def turn(s, first):
                for t in range(2):
                    pool.wait_ge(idx_in[t], 16 * (s + 1))
                    if not first:
                        wait_transposed(pool, s - 1, t)
                    pool.sem_inc(tile_begun, 1)
                    for f in range(NC):
                        pool.indirect_dma_start(
                            out=rows[t][:, f + 1, :], out_offset=None, in_=tables[f],
                            in_offset=bass.IndirectOffsetOnAxis(ap=idx[t][:, f:f + 1], axis=0),
                        ).then_inc(gathered[t], 16)

            turn(0, True)
            with pool.Fori(1, TURNS) as s:
                turn(s, False)

        @block.vector
        def _(dve):
            def compare(s, f, first):
                dve.wait_ge(spread, NH * s + f - f % 2 + 2)
                if f >= SLOTS:
                    wait_front(dve, front, s, "hot", f - SLOTS)
                elif not first:
                    wait_front(dve, front, s - 1, "hot", f + NH - SLOTS)
                ids_b = psum[0:HP_ROWS, IP[f // 2 % 2], (f % 2) * SB:(f % 2 + 1) * SB]
                nc.vector.tensor_tensor(
                    onehot[f % SLOTS][0:HP_ROWS, :, :],
                    ids_b.rearrange("p (o b) -> p o b", o=1).to_broadcast([HP_ROWS, HC, SB]),
                    hot_rows_sb[0:HP_ROWS, :].rearrange("p (c o) -> p c o", o=1).to_broadcast(
                        [HP_ROWS, HC, SB]),
                    ALU.is_equal).then_inc(compared, 1)

            def copy(o, x):
                return nc.vector.tensor_copy(o, x)

            def rest(f):
                dve.wait_ge(hot_rounded, f + 1)
                nc.vector.tensor_tensor(hot_lo[0:HP_ROWS, f, :, :].rearrange("p c d -> p (c d)"), raw[f % SLOTS],
                                        hot_hi[0:HP_ROWS, f, :, :].rearrange("p c d -> p (c d)").bitcast(fp32),
                                        ALU.subtract).then_inc(hot_split, 1)

            def rest_of_w1(half):
                a, b = W1_HALVES[half]
                dve.wait_ge(w1_rounded, half + 1)
                nc.vector.tensor_tensor(w1_lo[:, a:b, :].rearrange("p c n -> p (c n)"), raw_w1,
                                        w1_hi[:, a:b, :].rearrange("p c n -> p (c n)").bitcast(fp32),
                                        ALU.subtract).then_inc(w1_split, 1)

            def rest_of_pairs(s):
                for c in range(ZC):
                    dve.wait_ge(pairs_rounded, ZC * s + c + 1)
                    nc.vector.tensor_tensor(pairs_lo[0:FILL[c], c, :], pairs[0:FILL[c], c, :],
                                            pairs_hi[0:FILL[c], c, :].bitcast(fp32),
                                            ALU.subtract).then_inc(pairs_split, 1)

            def rest_of_dense(s):
                dve.wait_ge(dense_rounded, s + 1)
                nc.vector.tensor_tensor(dense_lo[:, :, :, :].rearrange("d s t k -> d t s k"),
                                        feats[:, :, :, 0].rearrange("d t (s k) -> d t s k", s=4),
                                        dense_hi[:, :, :, :].bitcast(fp32).rearrange("d s t k -> d t s k"),
                                        ALU.subtract).then_inc(dense_out, 1)

            def turn(s, first, last):
                for f in range(SLOTS, NH):
                    if first:
                        rest(f)
                    compare(s, f, first)
                if first:
                    rest_of_w1(0)
                else:
                    rest_of_pairs(s - 1)
                if last:
                    copy_gram(dve, copy, 1, s, 0, first)
                    copy_gram(dve, copy, 1, s, 1, first)
                    rest_of_dense(s)
                    return
                for f in (0, 1):
                    compare(s + 1, f, False)
                copy_gram(dve, copy, 1, s, 0, first)
                for f in (2, 3):
                    compare(s + 1, f, False)
                if first:
                    rest_of_w1(1)
                rest_of_dense(s)
                copy_gram(dve, copy, 1, s, 1, first)

            dve.wait_ge(ids_in, 16)
            nc.vector.tensor_copy(hot_ids_sb[:, :], raw_ids).then_inc(ids_cast, 1)
            dve.wait_ge(consts_in, 16 * 3)
            for f in range(SLOTS):
                rest(f)
                compare(0, f, True)
            turn(0, True, False)
            with dve.Fori(1, TURNS - 1) as s:
                turn(s, False, False)
            turn(TURNS - 1, False, True)
            rest_of_pairs(TURNS - 1)

        @block.scalar
        def _(act):
            def copy(o, x):
                return nc.scalar.activation(o, x, ACT.Copy)

            def round_hot(f):
                act.wait_ge(raw_in[f % SLOTS], 16 * (f // SLOTS + 1))
                copy(hot_hi[0:HP_ROWS, f, :, :].rearrange("p c d -> p (c d)"), raw[f % SLOTS]).then_inc(hot_rounded, 1)

            def round_w1(half):
                a, b = W1_HALVES[half]
                act.wait_ge(raw_w1_in, 16 * (half + 1))
                copy(w1_hi[:, a:b, :].rearrange("p c n -> p (c n)"), raw_w1).then_inc(w1_rounded, 1)

            def round_pairs(s):
                act.wait_ge(pairs_in, MOVED * (s + 1))
                for c in range(ZC):
                    copy(pairs_hi[0:FILL[c], c, :], pairs[0:FILL[c], c, :]).then_inc(pairs_rounded, 1)

            def copy_hot(s, f):
                b, n = front_use("hot", f)
                act.wait_ge(front[b], FRONT * s + n)
                copy(feats[:, :, :, NR + f].rearrange("d t n -> d (t n)"),
                     psum[:, FP[b], 0:SB]).then_inc(front_out[b], 1)

            def copy_rows(s, t, g, first):
                w = min(4, NR - 4 * g)
                b, n = front_use("rows", t, g)
                act.wait_ge(front[b], FRONT * s + n)
                if g == 0 and not first:
                    act.wait_ge(dense_out, s)
                copy(feats[:, t, :, 4 * g:4 * g + w],
                     psum[:, FP[b], 0:w * P].rearrange("d (f n) -> d n f", f=w)).then_inc(front_out[b], 1)

            def round_dense(s):
                for t in range(2):
                    wait_front(act, front_out, s, "rows", t, 0)
                copy(dense_hi[:, :, :, :].rearrange("d s t k -> d t s k"),
                     feats[:, :, :, 0].rearrange("d t (s k) -> d t s k", s=4)).then_inc(dense_rounded, 1)

            def relu(dst, bias, bank, chunks):
                for n, c in enumerate(chunks):
                    nc.scalar.activation(dst[:, c, :], psum[:, bank, n * SB:(n + 1) * SB], ACT.Relu,
                                         bias=bias[:, c:c + 1]).then_inc(relu_out, 1)

            def layer1a(s):
                act.wait_ge(mlp_a, 2 * s + 1)
                relu(h1, b1_sb, HP[0], (0, 1))

            def layer1b(s):
                act.wait_ge(mlp_b, 2 * s + 1)
                relu(h1, b1_sb, HP[1], (2, 3))

            def layer2(s):
                act.wait_ge(mlp_a, 2 * s + 2)
                relu(h2, b2_sb, HP[0], (0, 1))

            def layer3(s):
                act.wait_ge(mlp_b, 2 * s + 2)
                copy(y[:, bass.ds(s * SB, SB)], psum[0:1, HP[1], 0:SB]).then_inc(y_out, 1)

            layers = {"1a": layer1a, "1b": layer1b, "2": layer2, "3": layer3}

            def turn(s, steps, first, last):
                for kind, *n in steps:
                    if kind == "hot":
                        if first and n[0] >= SLOTS - 1 and n[0] < NH - 1:
                            round_hot(n[0] + 1)
                        copy_hot(s, *n)
                        if first and n[0] == NH - 1:
                            round_w1(0)
                        if n[0] == NH - 1 and not first:
                            round_pairs(s - 1)
                    elif kind == "rows":
                        copy_rows(s, *n, first)
                    elif kind == "gram" and n[1] == 0:
                        copy_gram(act, copy, 0, s, n[0], first)
                        if first and n[0] == 0:
                            round_w1(1)
                    elif kind == "dense":
                        round_dense(s)
                    elif kind == "layer" and not first:
                        if last and n[0] == "3":
                            round_pairs(s)
                        layers[n[0]](s - 1)

            for f in range(SLOTS):
                round_hot(f)
            act.wait_ge(weights_in, 16 * 4)
            turn(0, STEPS, True, False)
            with act.Fori(1, TURNS - 1) as s:
                turn(s, STEPS, False, False)
            turn(TURNS - 1, LAST_STEPS, False, True)
            for layer in layers.values():
                layer(TURNS - 1)

        @block.tensor
        def _(pe):
            def spread_ids(s, f):
                nc.tensor.matmul(psum[0:HP_ROWS, IP[f // 2 % 2], (f % 2) * SB:(f % 2 + 1) * SB],
                                 pick_sb[:, f:f + 1].to_broadcast([NH, HP_ROWS]), hot_ids_sb[:, bass.ds(s * SB, SB)],
                                 start=True, stop=True).then_inc(spread, 1)

            def hot(s, f, first, last_turn):
                pe.wait_ge(compared, NH * s + f + 1)
                if first:
                    pe.wait_ge(hot_split, f + 1)
                b, n = front_use("hot", f)
                if not (first and n == 1):
                    pe.wait_ge(front_out[b], FRONT * s + n - 1)
                for part in (hot_hi, hot_lo):
                    for c in range(HC):
                        last = nc.tensor.matmul(psum[:, FP[b], 0:SB], part[0:HP_ROWS, f, c, :],
                                                onehot[f % SLOTS][0:HP_ROWS, c, :],
                                                start=(part is hot_hi and c == 0),
                                                stop=(part is hot_lo and c == HC - 1))
                last.then_inc(front[b], 1)
                if f % 2 == 1:
                    for n in (f + 3, f + 4):
                        if n < NH:
                            spread_ids(s, n)
                        elif not last_turn:
                            spread_ids(s + 1, n - NH)

            def transposes(s, t, g):
                if g == 0:
                    pe.wait_ge(dense_in[t], 16 * (s + 1))
                    pe.wait_ge(gathered[t], GATHERED * (s + 1))
                b, n = front_use("rows", t, g)
                pe.wait_ge(front_out[b], FRONT * s + n - 1)
                for f in range(4 * g, min(4 * g + 4, NR)):
                    last = nc.tensor.transpose(psum[:, FP[b], (f - 4 * g) * P:(f - 4 * g + 1) * P],
                                               rows[t][:, f, :], ident_sb[:, :])
                last.then_inc(front[b], 1)

            def grams(s, t, h, first):
                if h == 0:
                    wait_front(pe, front_out, s, "rows", t, GROUPS - 1)
                    wait_front(pe, front_out, s, *(("hot", NH - 1) if t == 0 else ("rows", 1, GROUPS - 2)))
                if not (first and t == 0):
                    pe.wait_ge(gram_out[h], 4 * (2 * s + t))
                for k in range(HALF_K):
                    for q in range(4):
                        n = 32 * q + HALF_K * h + k
                        last = nc.tensor.matmul(psum[32 * q:32 * q + NJ, GP[h], k * NJ:(k + 1) * NJ],
                                                feats[:, t, n, 0:NJ], feats[:, t, n, 1:NF],
                                                start=True, stop=True)
                last.then_inc(gram_done[h], 1)

            def layer1(half, done):
                for c in (2 * half, 2 * half + 1):
                    o = psum[:, HP[half], (c % 2) * SB:(c % 2 + 1) * SB]
                    x = [tuple(x[:, :, :, :].rearrange("d s t k -> d (s t k)") for x in (dense_hi, dense_lo))]
                    x += [(pairs_hi[0:FILL[z], z, :], pairs_lo[0:FILL[z], z, :]) for z in range(ZC)]
                    for n, (x_hi, x_lo) in enumerate(x):
                        z = (n - 1) % (ZC + 1)
                        rows_in = D if n == 0 else FILL[z]
                        w_hi, w_lo = (w[0:rows_in, z, c * P:(c + 1) * P] for w in (w1_hi, w1_lo))
                        nc.tensor.matmul(o, w_hi, x_hi, start=(n == 0), stop=False)
                        nc.tensor.matmul(o, w_hi, x_lo, start=False, stop=False)
                        last = nc.tensor.matmul(o, w_lo, x_hi, start=False, stop=(n == ZC))
                last.then_inc(done, 1)

            def layer1a(s):
                pe.wait_ge(pairs_split, ZC * (s + 1))
                pe.wait_ge(dense_out, s + 1)
                pe.wait_ge(w1_split, 2)
                if not (isinstance(s, int) and s == 0):
                    pe.wait_ge(relu_out, RELUS * s)
                layer1(0, mlp_a)

            def layer1b(s):
                if not (isinstance(s, int) and s == 0):
                    pe.wait_ge(y_out, s)
                layer1(1, mlp_b)

            def layer2(s):
                pe.wait_ge(relu_out, RELUS * s + 2)
                for m in range(C2):
                    for c in range(C1):
                        if m == 0 and c > 1:
                            pe.wait_ge(relu_out, RELUS * s + c + 1)
                        last = nc.tensor.matmul(psum[:, HP[0], m * SB:(m + 1) * SB],
                                                w2_sb[:, c, m * P:(m + 1) * P], h1[:, c, :],
                                                start=(c == 0), stop=(c == C1 - 1))
                last.then_inc(mlp_a, 1)

            def layer3(s):
                pe.wait_ge(relu_out, RELUS * (s + 1))
                for m in range(C2):
                    last = nc.tensor.matmul(psum[0:1, HP[1], 0:SB], w3_sb[:, m:m + 1], h2[:, m, :],
                                            start=(m == 0), stop=(m == C2 - 1))
                last.then_inc(mlp_b, 1)

            layers = {"1a": layer1a, "1b": layer1b, "2": layer2, "3": layer3}

            def turn(s, steps, first, last_turn):
                for kind, *n in steps:
                    if kind == "hot":
                        hot(s, *n, first, last_turn)
                    elif kind == "rows":
                        transposes(s, *n)
                    elif kind == "gram":
                        grams(s, *n, first)
                    elif kind == "layer" and not first:
                        layers[n[0]](s - 1)

            pe.wait_ge(consts_in, 16 * 3)
            pe.wait_ge(ids_cast, 1)
            for f in range(4):
                spread_ids(0, f)
            turn(0, STEPS, True, False)
            pe.wait_ge(weights_in, 16 * 4)
            with pe.Fori(1, TURNS - 1) as s:
                turn(s, STEPS, False, False)
            turn(TURNS - 1, LAST_STEPS, False, True)
            layer1a(TURNS - 1)
            layer1b(TURNS - 1)
            layer2(TURNS - 1)
            layer3(TURNS - 1)


def pair_pieces(nf):
    blocks, top = [], nf - 1
    while top > 0:
        w = min(3, top)
        blocks.append((top, top - w + 1, w))
        top -= w
    size = [n * w for n, _, w in blocks]

    def place(fill, at):
        if at == len(blocks):
            return []
        for c in range(len(fill)):
            if fill[c] + size[at] <= 128:
                rest = place(fill[:c] + [fill[c] + size[at]] + fill[c + 1:], at + 1)
                if rest is not None:
                    return [c] + rest
        return None

    chunks = -(-sum(size) // 128)
    while (placed := place([0] * chunks, 0)) is None:
        chunks += 1
    fill, pieces = [0] * chunks, []
    for c, (n, j0, w) in zip(placed, blocks):
        pieces.append((c, fill[c], n, j0, w))
        fill[c] += n * w
    return pieces, fill


def kernel(**inputs):
    import numpy as np
    import concourse.bacc as bacc
    from concourse.bass_utils import run_bass_kernel_spmd

    ids = np.asarray(inputs["ids"])
    dense = np.asarray(inputs["r_dense_features"])
    w1 = np.asarray(inputs["W_top1"])
    tables = [np.asarray(inputs[f"tbl_{f}"]) for f in range(ids.shape[1])]
    batch, d = dense.shape
    nf = len(tables) + 1

    hot = [f for f, x in enumerate(tables) if x.shape[0] == 1000][:NUM_HOT]
    cold = [f for f in range(len(tables)) if f not in hot]
    order = [0] + [f + 1 for f in cold + hot]

    def by_tile(a):
        return a.reshape(batch // 256, 4, 2, 32, -1).transpose(0, 2, 1, 3, 4).reshape(batch // 128, 128, -1)

    pieces, fill = pair_pieces(nf)
    rows = np.full((len(fill) + 1, 128), -1)
    row_of = {(i, j): n for n, (i, j) in enumerate(zip(*np.triu_indices(nf, 1)))}
    for c, p0, n, j0, w in pieces:
        for i in range(n):
            for j in range(j0, j0 + w):
                if i < j:
                    rows[c, p0 + w * i + j - j0] = row_of[tuple(sorted((order[i], order[j])))]
    rows[-1, :d] = len(row_of) + np.arange(d)
    padded = np.concatenate([w1, np.zeros((1, w1.shape[1]), w1.dtype)])
    by_tiles = by_tile(ids)
    arrays = {
        "ids": by_tiles[:, :, cold],
        "dense": by_tile(dense),
        "ident": np.eye(128, dtype=np.float32),
        "hot_ids": by_tiles[:, :, hot].transpose(2, 0, 1).reshape(len(hot), batch),
        "hot_rows": np.arange(1000, dtype=np.float32).reshape(125, 8),
        "pick": np.eye(len(hot), dtype=np.float16),
        "w1": padded[rows.ravel()],
        "b1": np.asarray(inputs["b_top1"]).reshape(-1, 128).T,
        "w2": np.asarray(inputs["W_top2"]),
        "b2": np.asarray(inputs["b_top2"]).reshape(-1, 128).T,
        "w3": np.asarray(inputs["W_top3"]).reshape(-1, 128).T,
    }
    for f, x in enumerate(tables):
        arrays[f"table{f}"] = x
    arrays = {k: np.ascontiguousarray(v) for k, v in arrays.items()}

    nc = bacc.Bacc("TRN2", target_bir_lowering=False, num_devices=1)
    ap = {k: nc.dram_tensor(k, v.shape, mybir.dt.from_np(v.dtype), kind="ExternalInput").ap()
          for k, v in arrays.items()}
    out = nc.dram_tensor("out", (1, batch), mybir.dt.float32, kind="ExternalOutput").ap()
    dlrm_tower(nc, ap["ids"], ap["dense"], [ap[f"table{f}"] for f in cold], ap["ident"], ap["hot_ids"],
               [ap[f"table{f}"] for f in hot], ap["hot_rows"], ap["pick"],
               ap["w1"], ap["b1"], ap["w2"], ap["b2"], ap["w3"], out)
    r = run_bass_kernel_spmd(nc, [arrays], core_ids=[0])
    return r.results[0]["out"].reshape(batch, 1)
```
